# Optimizing a Trainium2 kernel written in Bass

```python
import numpy as np
import jax
import jax.numpy as jnp

def _softmax(x, axis=-1):
    return jax.nn.softmax(x, axis=axis)

def _gelu(x):
    return jax.nn.gelu(x, approximate=True)

def _silu(x):
    return jax.nn.silu(x)

def _sigmoid(x):
    return jax.nn.sigmoid(x)

def _layernorm(x, axis=-1, eps=1e-05):
    m = jnp.mean(x, axis=axis, keepdims=True)
    v = jnp.var(x, axis=axis, keepdims=True)
    return (x - m) / jnp.sqrt(v + eps)

def _scatter_add(tgt, idx, src, axis=0):
    return tgt.at[idx].add(src)

def _segment_sum(src, seg, n):
    return jax.ops.segment_sum(src, seg, n)
kernel_name = 'mk_xattn_seq_d1_seqx_r8_c16d22'

def setup_inputs(seed: int=0):
    np.random.seed(seed)
    _w = jnp.asarray

    def _rec_inputs():
        import jax
        import jax.numpy as jnp
        _rk = jax.random.key(seed)
        x = -0.0002928 + 1 * jax.random.normal(jax.random.fold_in(_rk, 1), (128, 64, 128), jnp.float32)
        _lenS = 64 - jax.random.randint(jax.random.fold_in(_rk, 7), (128,), 0, max(1, 64 // 4) + 1, jnp.int32)
        _lenS2 = 64 - jax.random.randint(jax.random.fold_in(_rk, 8), (128,), 0, max(1, 64 // 4) + 1, jnp.int32)
        _ctx_1024P = jax.random.normal(jax.random.fold_in(_rk, 11), (128, 16, 128), jnp.float32)
        _ctx_1024c = jax.random.dirichlet(jax.random.fold_in(_rk, 511), 0.3 * jnp.ones((16,), jnp.float32), (128, 64))
        _ctx_1024t = jnp.einsum('bsk,bkd->bsd', _ctx_1024c, _ctx_1024P)
        _ctx_1024t = _ctx_1024t * jax.lax.rsqrt(jnp.mean(jnp.square(_ctx_1024t)) + 1e-12) * 0.953939
        ctx_1024 = -1.39393e-06 + 0.999914 * (_ctx_1024t + 0.3 * jax.random.normal(jax.random.fold_in(_rk, 611), (128, 64, 128), jnp.float32))
        _validS = jnp.arange(64)[None, :] < _lenS[:, None]
        _validS2 = jnp.arange(64)[None, :] < _lenS2[:, None]
        _causal = jnp.tril(jnp.ones((64, 64), dtype=bool))
        mask_BxS2_ff1 = jnp.where(jnp.ones((128, 64), dtype=bool), 1.0, 0.0).astype(jnp.float32)
        return (x, ctx_1024, mask_BxS2_ff1)
    x, ctx_1024, mask_BxS2_ff1 = _rec_inputs()

    def _L0_xattn_setup():
        import jax, jax.numpy as jnp
        import numpy as np
        B, SEG, MEM, MODEL, H, D = (8, 64, 64, 128, 16, 64)
        TOT = SEG + MEM
        W_SCALE = 0.03
        key = jax.random.key(seed)
        ks = jax.random.split(key, 10)
        return {'x': jax.random.normal(ks[0], (B, SEG, MODEL), jnp.float32), 'mem': jax.random.normal(ks[1], (B, MEM, MODEL), jnp.float32), 'att_mask': jnp.ones((B, SEG), jnp.float32), 'w_q': jax.random.normal(ks[2], (MODEL, H * D), jnp.float32) * W_SCALE, 'w_k': jax.random.normal(ks[3], (MODEL, H * D), jnp.float32) * W_SCALE, 'w_v': jax.random.normal(ks[4], (MODEL, H * D), jnp.float32) * W_SCALE, 'w_r': jax.random.normal(ks[5], (MODEL, H * D), jnp.float32) * W_SCALE, 'mlp_w': jax.random.normal(ks[6], (H * D, MODEL), jnp.float32) * W_SCALE, 'u1': jax.random.normal(ks[7], (1, H, 1, D), jnp.float32), 'u2': jax.random.normal(ks[8], (1, H, 1, D), jnp.float32), 'R': jax.random.normal(ks[9], (TOT, MODEL), jnp.float32), 'ln_gamma': jnp.ones((MODEL,), jnp.float32), 'ln_beta': jnp.zeros((MODEL,), jnp.float32)}
    _L0_xattn_all = _L0_xattn_setup()
    _L0_xattn_in = {k: v for k, v in _L0_xattn_all.items() if k in ('w_q', 'w_k', 'w_v', 'w_r', 'mlp_w', 'u1', 'u2', 'R', 'ln_gamma', 'ln_beta')}
    del _L0_xattn_all
    return {'x': x, 'ctx_1024': ctx_1024, 'mask_BxS2_ff1': mask_BxS2_ff1, 'L0_xattn_w_q': _L0_xattn_in['w_q'], 'L0_xattn_w_k': _L0_xattn_in['w_k'], 'L0_xattn_w_v': _L0_xattn_in['w_v'], 'L0_xattn_w_r': _L0_xattn_in['w_r'], 'L0_xattn_mlp_w': _L0_xattn_in['mlp_w'], 'L0_xattn_u1': _L0_xattn_in['u1'], 'L0_xattn_u2': _L0_xattn_in['u2'], 'L0_xattn_R': _L0_xattn_in['R'], 'L0_xattn_ln_gamma': _L0_xattn_in['ln_gamma'], 'L0_xattn_ln_beta': _L0_xattn_in['ln_beta']}

def reference(x, ctx_1024, mask_BxS2_ff1, L0_xattn_w_q, L0_xattn_w_k, L0_xattn_w_v, L0_xattn_w_r, L0_xattn_mlp_w, L0_xattn_u1, L0_xattn_u2, L0_xattn_R, L0_xattn_ln_gamma, L0_xattn_ln_beta):
    import jax
    import jax.numpy as jnp

    def _L0_xattn_ref(x, mem, att_mask, w_q, w_k, w_v, w_r, mlp_w, u1, u2, R, ln_gamma, ln_beta):
        import jax, jax.numpy as jnp
        import numpy as np
        B, SEG, MEM, MODEL, H, D = (8, 64, 64, 128, 16, 64)
        TOT = SEG + MEM
        W_SCALE = 0.03
        h = jnp.concatenate([mem, x], axis=1)
        b, seg_len, model = x.shape
        total = h.shape[1]
        mem_len = total - seg_len
        nh, d = (u1.shape[1], u1.shape[3])
        q = (x @ w_q).reshape(b, nh, seg_len, d)
        k = (h @ w_k).reshape(b, nh, total, d)
        v = (h @ w_v).reshape(b, nh, total, d)
        r = (R[-total:] @ w_r).reshape(1, nh, total, d)
        ac = jnp.einsum('bhid,bhjd->bhij', q + u1, k)
        bd = jnp.einsum('bhid,bhjd->bhij', q + u2, r)
        i_idx = jnp.arange(seg_len)[:, None]
        j_idx = jnp.arange(total)[None, :]
        shift_idx = (j_idx - i_idx + seg_len - 1) % total
        bd = bd[:, :, i_idx, shift_idx]
        s = ac + bd
        causal = j_idx - i_idx <= mem_len
        s = jnp.where(causal, s, 0.0) / d ** 0.5
        s = jnp.where(s == 0.0, -jnp.inf, s)
        p = jax.nn.softmax(s, axis=-1)
        p = p * att_mask[:, None, :, None]
        att = (p @ v).reshape(b, seg_len, nh * d)
        out = att @ mlp_w
        y = out + x
        mu = jnp.mean(y, axis=-1, keepdims=True)
        var = jnp.mean((y - mu) ** 2, axis=-1, keepdims=True)
        return (y - mu) / jnp.sqrt(var + 1e-05) * ln_gamma + ln_beta
    x = _L0_xattn_ref(x, ctx_1024, mask_BxS2_ff1, L0_xattn_w_q, L0_xattn_w_k, L0_xattn_w_v, L0_xattn_w_r, L0_xattn_mlp_w, L0_xattn_u1, L0_xattn_u2, L0_xattn_R, L0_xattn_ln_gamma, L0_xattn_ln_beta)
    return x

_drawn_inputs = setup_inputs


def setup_inputs(seed=0):
    import zlib

    import numpy as np

    out = dict(_drawn_inputs(seed))
    spreads = {'L0_xattn_ln_gamma': (1.0, 0.2), 'L0_xattn_ln_beta': (0.0, 0.1)}
    factors = {'L0_xattn_w_q': 8.0,
     'L0_xattn_w_k': 3.731,
     'L0_xattn_w_r': 4.312,
     'L0_xattn_u1': 3.956,
     'L0_xattn_u2': 4.707,
     'L0_xattn_R': 4.326}
    for name, (base, spread) in spreads.items():
        noise = np.random.default_rng([zlib.crc32(name.encode()), seed]).standard_normal(out[name].shape)
        drawn = base * np.exp(spread * noise) if base else spread * noise
        out[name] = jnp.asarray(drawn.astype(out[name].dtype))
    for name, factor in factors.items():
        out[name] = (out[name] * factor).astype(out[name].dtype)
    return out
```

```python
from contextlib import ExitStack

import concourse.bass as bass
from concourse import mybir


def xattn_program(nc, x, h, mask, w_q, w_k, w_v, w_r, mlp_w, u1, u2, R, gamma, beta, out):
    F32, F32R = mybir.dt.float32, mybir.dt.float32r
    ALU = mybir.AluOpType
    ACT = mybir.ActivationFunctionType
    AX = mybir.AxisListType

    B, SEG, MODEL = x.shape
    TOT = h.shape[1]
    NH, D = u1.shape
    XR, HR = SEG // NH, TOT // NH
    NB = NH * D // D
    NC = NB // 2
    PAIRS = B // 2
    HP = PAIRS // 2
    GP = 4
    GROUPS = PAIRS // GP
    BANK = 512
    HALF = 64
    SHRINK = 2.0**-40
    EXP_SCALE = -(1.0 / SHRINK) / D**0.5
    EPS = 1e-5
    WIN = TOT + SEG

    TOKENS = [("tokens", k) for k in range(3)]
    FOLD = [("fold", k) for k in range(4)]
    POSVAL = []
    for k in range(16):
        POSVAL += [("pos", (k % XR, k // XR)), ("val", (k // 2, k % 2))]
    KEYS = [[("key", (g, c)) for c in range(NC)] + [("query", (g, c)) for c in range(NC // 2)] for g in range(2)]
    NEXT = TOKENS + FOLD + POSVAL + KEYS[0]
    OUT = [("out", 0)]
    PROLOGUE = [NEXT]
    LAG_T, LAG_V = 2, 3
    SLOTS = GROUPS + LAG_V

    def spread(last):
        slots = [[] for _ in range(SLOTS)]
        for k, job in enumerate(KEYS[1]):
            slots[k // 2].append(job)
        if not last:
            slots[6] += TOKENS[:2]
            slots[7] += TOKENS[2:] + FOLD[:3]
            rest = FOLD[3:] + POSVAL + KEYS[0]
            for k, job in enumerate(rest):
                slots[8 + k * (SLOTS - 8) // len(rest)].append(job)
        slots[-1] += OUT
        return slots

    BODY, LAST = spread(False), spread(True)
    ON_ACT = ("tokens", "fold", "val", "key", "query")
    ON_DVE = ("tokens", "fold", "pos", "key", "query", "out")

    def count(slots, kinds, end=None):
        return sum(k in kinds for k, _ in sum(slots, [])[:end])

    ALL = ON_ACT + ON_DVE
    PRO_JOBS, BODY_JOBS = count(PROLOGUE, ALL), count(BODY, ALL)
    PRO_ACT, BODY_ACT = count(PROLOGUE, ON_ACT), count(BODY, ON_ACT)
    PRO_DVE, BODY_DVE = count(PROLOGUE, ON_DVE), count(BODY, ON_DVE)
    RINGS = 4
    assert BODY_JOBS % RINGS == 0
    PRO_BANK = -PRO_JOBS % RINGS

    def jobs_before(n):
        return 0 if isinstance(n, int) and n < 0 else n * BODY_JOBS + PRO_JOBS

    def act_before(n):
        return 0 if isinstance(n, int) and n < 0 else n * BODY_ACT + PRO_ACT

    def dve_before(n):
        return 0 if isinstance(n, int) and n < 0 else n * BODY_DVE + PRO_DVE

    def numbered(slots, first_bank=0):
        at, result = 0, []
        for jobs in slots:
            result.append([(at + k, (first_bank + at + k) % RINGS, *job) for k, job in enumerate(jobs)])
            at += len(jobs)
        return result

    with ExitStack() as ctx:

        def sb(name, shape, dt=F32):
            return ctx.enter_context(nc.sbuf_tensor(name, shape, dt))

        def sem(name):
            return ctx.enter_context(nc.semaphore(name))

        wq = sb("wq", [128, NC * 128])
        wqT = sb("wqT", [128, NC, MODEL])
        wk_hi, wk_lo = sb("wk_hi", [128, NC * 128], F32R), sb("wk_lo", [128, NC * 128], F32R)
        wv_hi, wv_lo = sb("wv_hi", [128, NC * 128], F32R), sb("wv_lo", [128, NC * 128], F32R)
        mlp = sb("mlp", [128, NC, MODEL])
        rT = sb("rT", [128, NH * TOT])
        r_diag = sb("r_diag", [128, 2 * TOT])
        fold_hi, fold_lo = sb("fold_hi", [128, NB * TOT + SEG], F32R), sb("fold_lo", [128, NB * TOT + SEG], F32R)
        u2r = sb("u2r", [128, WIN])
        gamma_b, beta_b = sb("gamma_b", [128, MODEL]), sb("beta_b", [128, MODEL])
        ident = sb("ident", [128, 128])
        u1s, u2T = sb("u1s", [128, NH]), sb("u2T", [128, NH])
        mask_i = sb("mask_i", [128, PAIRS])
        power, epsilon = sb("power", [128, XR]), sb("epsilon", [128, XR])
        u1_head = sb("u1_head", [128, 1])
        x_tok, h_tok = sb("x_tok", [128, XR * MODEL]), sb("h_tok", [128, HR * MODEL])
        x_res = sb("x_res", [128, XR * MODEL])
        xT = sb("xT", [128, XR * B])
        xT_hi, xT_lo = sb("xT_hi", [128, XR * B], F32R), sb("xT_lo", [128, XR * B], F32R)
        hT_hi, hT_lo = sb("hT_hi", [128, HR * B], F32R), sb("hT_lo", [128, HR * B], F32R)
        kT = [sb(f"kT{g}", [128, HP * TOT]) for g in range(2)]
        q_diag = [sb(f"q_diag{g}", [128, HP * 128]) for g in range(2)]
        pos_out = [sb(f"pos_out{k}", [128, BANK]) for k in range(4)]
        val_out = [sb(f"val_out{k}", [128, BANK]) for k in range(4)]
        pos_in = [sb(f"pos_in{k}", [128, GP * TOT]) for k in range(4)]
        val_in = [sb(f"val_in{k}", [128, 2, GP, D]) for k in range(4)]
        prob = [sb(f"prob{k}", [128, GP * TOT]) for k in range(4)]
        probT = [sb(f"probT{k}", [128, GP, 128]) for k in range(2)]
        least = sb("least", [128, 4, GP])
        shift = sb("shift", [128, 4, GP])
        total = sb("total", [128, 4, GP])
        inverse = sb("inverse", [128, 4, GP])
        weight = sb("weight", [128, 4, GP])
        attT = sb("attT", [128, NC, XR, B])
        y = sb("y", [128, XR * MODEL])
        stats, mean_var = sb("stats", [128, XR, 6]), sb("mean_var", [128, XR, 2])
        rstd = sb("rstd", [128, XR])

        psum = ctx.enter_context(nc.psum_tensor("psum", [128, 8, BANK], F32))
        score_bank = [psum[:, k, :] for k in range(2)]
        prob_bank = psum[:, 2, :]
        att_bank = psum[:, 3, :]
        job_bank = [psum[:, 4 + k, :] for k in range(RINGS)]

        pos_dram = nc.dram_tensor("pos_dram", (NH, B, SEG * TOT), F32, kind="Internal").ap()
        val_dram = nc.dram_tensor("val_dram", (NH, B, TOT * D), F32, kind="Internal").ap()
        u2r_dram = nc.dram_tensor("u2r_dram", (1, NH * TOT), F32, kind="Internal").ap()

        wk_raw, wv_raw, wr_raw = (kT[0][:, k * 1024:(k + 1) * 1024] for k in range(3))
        R_tok = kT[0][:, 3072:3200]
        u1_rows, u2_rows = kT[0][0:NH, 3200:3328], kT[0][0:NH, 3328:3456]
        mask_tok = kT[0][:, 3456:3520]
        wr_twice = kT[1][:, 0:2048]
        RT = kT[1][:, 2048:2176]
        u2r_row = kT[1][0:1, 0:NH * TOT]

        setup_loaded = sem("setup_loaded")
        gammas_loaded = sem("gammas_loaded")
        ident_zero, ident_ready = sem("ident_zero"), sem("ident_ready")
        pool_fills, dve_fills = sem("pool_fills"), sem("dve_fills")
        weights_high, weights_split = sem("weights_high"), sem("weights_split")
        setup_products, setup_copied = sem("setup_products"), sem("setup_copied")
        u2r_stored = sem("u2r_stored")

        x_loaded, h_loaded, u2r_loaded, res_loaded = sem("x_loaded"), sem("h_loaded"), sem("u2r_loaded"), sem("res_loaded")
        diag_ready, u1_ready = sem("diag_ready"), sem("u1_ready")
        job_done, job_act, job_dve = sem("job_done"), sem("job_act"), sem("job_dve")
        pos_stored, val_stored = [sem(f"pos_stored{k}") for k in range(4)], [sem(f"val_stored{k}") for k in range(4)]
        pos_loaded, val_loaded = [sem(f"pos_loaded{k}") for k in range(4)], [sem(f"val_loaded{k}") for k in range(4)]
        scores_done, scores_added, scores_marked = sem("scores_done"), sem("scores_added"), sem("scores_marked")
        least_done, shift_done, exp_done = sem("least_done"), sem("shift_done"), sem("exp_done")
        inverse_done, weight_done, prob_done = sem("inverse_done"), sem("weight_done"), sem("prob_done")
        transposed, probT_done, values_done = sem("transposed"), sem("probT_done"), sem("values_done")
        att_act, att_dve = sem("att_act"), sem("att_dve")
        stats_done, aggr_done = sem("stats_done"), sem("aggr_done")
        norm_steps, y_stored = sem("norm_steps"), sem("y_stored")
        NORM_STEPS = 6
        SETUP_LOADS = 11

        x_rows = x.rearrange("b s m -> b (s m)")
        h_rows = h.rearrange("b s m -> b (s m)")
        out_rows = out.rearrange("b s m -> b (s m)")

        def rows(array, n, width):
            return array[:, bass.ds(n * width, width)]

        def key_cols(g, half, c, e):
            view = kT[g][HALF * half:HALF * (half + 1), :].rearrange("k (p t c e) -> k p t c e", t=HR, c=NC, e=2)
            return view[:, :, :, c, e].rearrange("k p t -> k t p")

        def query_cols(g, half, cc, f):
            view = q_diag[g][HALF * half:HALF * (half + 1), :].rearrange(
                "k (p z s c q f) -> k p z s c q f", z=2, s=XR, c=NC // 2, q=2, f=2)
            return view[:, :, half, :, cc, :, f].rearrange("k p s q -> k q s p")

        def att_cols(g, half, f):
            b = HALF * half + GP * g
            return attT[HALF * f:HALF * (f + 1), :, :, b:b + GP].rearrange("k a s b -> k b s a")

        def att_from(half, f):
            view = att_bank[HALF * half:HALF * (half + 1), 0:GP * SEG].rearrange("k (b s a f) -> k b s a f", b=GP, s=XR, f=2)
            return view[:, :, :, :, f]

        def window(tile, width, start, step):
            return bass.AP(tile[:, :].tensor, start, [[width, 128], [step, 4], [1, TOT]])

        block = ctx.enter_context(nc.Block())

        @block.sync
        def _(sp):
            loads = [
                (wq[:, :], w_q), (wk_raw, w_k), (wv_raw, w_v), (wr_raw, w_r),
                (mlp[:, :, :], mlp_w.rearrange("(c p) m -> p c m", p=128)), (R_tok, R),
                (u1_rows[:, 0:D], u1), (u1_rows[:, D:2 * D], u1), (u2_rows[:, 0:D], u2), (u2_rows[:, D:2 * D], u2),
                (mask_tok, mask),
            ]
            for dst, src in loads:
                sp.dma_start(dst, src).then_inc(setup_loaded, 16)
            sp.dma_start(gamma_b[:, :], gamma.partition_broadcast(128)).then_inc(gammas_loaded, 16)
            sp.dma_start(beta_b[:, :], beta.partition_broadcast(128)).then_inc(gammas_loaded, 16)
            sp.sem_inc(y_stored, 16)

            def load_tokens(n):
                sp.dma_start(x_tok[:, :], rows(x_rows, n, XR * MODEL)).then_inc(x_loaded, 16)
                sp.dma_start(h_tok[:, :], rows(h_rows, n, HR * MODEL)).then_inc(h_loaded, 16)

            def load_u2r(n):
                sp.dma_start(u2r[:, 0:TOT], u2r_dram[0:1, bass.ds(n * TOT, TOT)].partition_broadcast(128)).then_inc(u2r_loaded, 16)

            def store_jobs(n, slots, jobs):
                for at, _, kind, what in jobs:
                    if kind == "pos":
                        s, ag = what
                        k = s + XR * ag
                        sp.wait_ge(job_dve, dve_before(n) + count(slots, ON_DVE, at + 1))
                        dst = pos_dram[bass.ds(n + 1, 1), :, (16 * s + 4 * ag) * TOT:(16 * s + 4 * ag + 4) * TOT]
                        sp.dma_start(dst.rearrange("o b c -> (o b) c"), pos_out[k % 4][:, :]).then_inc(pos_stored[k % 4], 16)
                    if kind == "val":
                        t, vh = what
                        k = 2 * t + vh
                        sp.wait_ge(job_act, act_before(n) + count(slots, ON_ACT, at + 1))
                        dst = val_dram[bass.ds(n + 1, 1), :, k * BANK:(k + 1) * BANK]
                        sp.dma_start(dst.rearrange("o b c -> (o b) c"), val_out[k % 4][:, :]).then_inc(val_stored[k % 4], 16)

            def load_pos(n, g):
                for half in range(2):
                    b = HALF * half + GP * g
                    src = pos_dram[bass.ds(n, 1), b:b + GP, :].rearrange("o p (i j) -> (o i) p j", j=TOT)
                    dst = pos_in[g % 4][HALF * half:HALF * (half + 1), :].rearrange("i (p j) -> i p j", j=TOT)
                    sp.dma_start(dst, src).then_inc(pos_loaded[g % 4], 16)

            def load_val(n, g):
                for half in range(2):
                    if half == 1 and g == GROUPS - 1:
                        sp.wait_ge(scores_added, n * GROUPS + g)
                    b = HALF * half + GP * g
                    src = val_dram[bass.ds(n, 1), b:b + GP, :].rearrange("o p (j d) -> (o j) p d", d=D)
                    sp.dma_start(val_in[g % 4][:, half, :, :], src).then_inc(val_loaded[g % 4], 16)

            load_tokens(0)
            sp.wait_ge(setup_copied, 3)
            sp.dma_start(u2r_dram, u2r_row).then_inc(u2r_stored, 16)
            sp.wait_ge(u2r_stored, 16)
            load_u2r(0)
            store_jobs(-1, PROLOGUE, numbered(PROLOGUE, PRO_BANK)[0])
            for k in range(4):
                sp.wait_ge(pos_stored[k], 64)
            for g in range(3):
                load_pos(0, g)

            def head(n, last):
                if not last:
                    load_tokens(n + 1)
                    load_u2r(n + 1)
                sp.dma_start(x_res[:, :], rows(x_rows, n, XR * MODEL)).then_inc(res_loaded, 16)
                for k in range(4):
                    sp.wait_ge(val_stored[k], n * 64 + 64)
                slots = LAST if last else BODY
                for slot, jobs in enumerate(numbered(slots)):
                    if slot + 3 < GROUPS:
                        if slot >= 1:
                            sp.wait_ge(scores_added, n * GROUPS + slot)
                        load_pos(n, slot + 3)
                    if slot < GROUPS:
                        if slot >= 4:
                            sp.wait_ge(values_done, n * GROUPS + (slot - 3))
                        load_val(n, slot)
                    store_jobs(n, slots, jobs)
                if not last:
                    for k in range(4):
                        sp.wait_ge(pos_stored[k], n * 64 + 128)
                    for g in range(3):
                        load_pos(n + 1, g)
                sp.wait_ge(norm_steps, n * NORM_STEPS + NORM_STEPS)
                sp.dma_start(rows(out_rows, n, XR * MODEL), y[:, :]).then_inc(y_stored, 16)

            with sp.Fori(0, NH - 1) as n:
                head(n, False)
            head(NH - 1, True)
            sp.wait_ge(y_stored, 16 * (NH + 1))

        @block.gpsimd
        def _(pool):
            nc.gpsimd.memset(ident[:, :], 0.0).then_inc(ident_zero, 1)
            pool.wait_ge(ident_zero, 1)
            nc.gpsimd.affine_select(out=ident[:, :], in_=ident[:, :], compare_op=ALU.not_equal, fill=1.0, base=0,
                                    pattern=[[-1, 128]], channel_multiplier=1).then_inc(ident_ready, 1)
            nc.gpsimd.memset(r_diag[:, :], 0.0).then_inc(pool_fills, 1)
            nc.gpsimd.memset(power[:, :], -0.5).then_inc(pool_fills, 1)
            nc.gpsimd.memset(epsilon[:, :], EPS).then_inc(pool_fills, 1)
            for g in range(2):
                nc.gpsimd.memset(q_diag[g][:, :], 0.0).then_inc(pool_fills, 1)

            def fill_diag(n):
                nc.gpsimd.tensor_copy(r_diag[0:HALF, 0:TOT], rT[0:HALF, bass.ds(n * TOT, TOT)])
                nc.gpsimd.tensor_copy(r_diag[HALF:, TOT:], rT[HALF:, bass.ds(n * TOT, TOT)]).then_inc(diag_ready, 1)
                pool.wait_ge(diag_ready, n + 1)

            def fill_u1(n):
                nc.gpsimd.tensor_copy(u1_head[:, :], u1s[:, bass.ds(n, 1)]).then_inc(u1_ready, 1)

            pool.wait_ge(setup_copied, 2)
            pool.wait_ge(pool_fills, 5)
            fill_diag(0)
            fill_u1(0)

            def head(n, last):
                for g in range(GROUPS):
                    if g == 4 and not last:
                        pool.wait_ge(prob_done, n * GROUPS + g)
                        fill_diag(n + 1)
                    if g == 10 and not last:
                        fill_u1(n + 1)
                    pool.wait_ge(weight_done, n * GROUPS + (g + 1))
                    p = prob[g % 4][:, :].rearrange("k (p j) -> k p j", j=TOT)
                    nc.gpsimd.tensor_tensor(p, p, weight[:, g % 4, :].unsqueeze(2).to_broadcast([128, GP, TOT]),
                                            ALU.mult).then_inc(prob_done, 1)

                y3 = y[:, :].rearrange("b (s m) -> b s m", m=MODEL)

                def step(k, instruction):
                    instruction.then_inc(norm_steps, 1)
                    if k < NORM_STEPS:
                        pool.wait_ge(norm_steps, n * NORM_STEPS + k)

                pool.wait_ge(aggr_done, n + 1)
                step(1, nc.gpsimd.tensor_tensor(rstd[:, :], mean_var[:, :, 1], epsilon[:, :], ALU.add))
                step(2, nc.gpsimd.tensor_tensor(rstd[:, :], rstd[:, :], power[:, :], ALU.pow))
                step(3, nc.gpsimd.tensor_tensor(y3, y3, mean_var[:, :, 0].unsqueeze(2).to_broadcast([128, XR, MODEL]), ALU.subtract))
                step(4, nc.gpsimd.tensor_tensor(y3, y3, rstd[:, :].unsqueeze(2).to_broadcast([128, XR, MODEL]), ALU.mult))
                pool.wait_ge(gammas_loaded, 32)
                step(5, nc.gpsimd.tensor_tensor(y3, y3, gamma_b[:, :].unsqueeze(1).to_broadcast([128, XR, MODEL]), ALU.mult))
                step(6, nc.gpsimd.tensor_tensor(y3, y3, beta_b[:, :].unsqueeze(1).to_broadcast([128, XR, MODEL]), ALU.add))

            with pool.Fori(0, NH - 1) as n:
                head(n, False)
            head(NH - 1, True)

        @block.scalar
        def _(act):
            act.wait_ge(setup_products, 1)
            for k in range(2):
                nc.scalar.activation(wqT[:, 4 * k:4 * k + 4, :], psum[:, k, :].rearrange("k (c m) -> k c m", c=4), ACT.Copy)
            nc.scalar.activation(RT, psum[:, 2, 0:128], ACT.Copy)
            nc.scalar.activation(u1s[:, :], psum[:, 2, 128:144], ACT.Copy, scale=SHRINK)
            nc.scalar.activation(u2T[:, :], psum[:, 2, 144:160], ACT.Copy)
            for half in range(2):
                last = nc.scalar.activation(mask_i[HALF * half:HALF * (half + 1), :],
                                            psum[0:SEG, 2, 160 + HALF * half:160 + HALF * (half + 1)], ACT.Copy)
            last.then_inc(setup_copied, 1)
            act.wait_ge(setup_products, 2)
            for k in range(4):
                dst = rT[:, :].rearrange("k (x b) -> k x b", b=NB)[:, :, 4 * k:4 * k + 4]
                last = nc.scalar.activation(dst, psum[:, 4 + k, :].rearrange("k (b x) -> k x b", b=4), ACT.Copy)
            last.then_inc(setup_copied, 1)
            act.wait_ge(setup_products, 3)
            for k in range(4):
                last = nc.scalar.activation(u2r_row[:, k * BANK:(k + 1) * BANK], psum[0:1, k, :], ACT.Copy, scale=SHRINK)
            last.then_inc(setup_copied, 1)

            def copy_jobs(n, slots, jobs):
                for at, bank, kind, what in jobs:
                    if kind not in ON_ACT:
                        continue
                    ps = job_bank[bank]
                    act.wait_ge(job_done, jobs_before(n) + (at + 1))
                    if kind == "tokens" and what == 0:
                        nc.scalar.activation(xT[:, :], ps, ACT.Copy)
                        last = nc.scalar.activation(xT_hi[:, :], ps, ACT.Copy)
                    if kind == "tokens" and what > 0:
                        last = nc.scalar.activation(hT_hi[:, (what - 1) * BANK:what * BANK], ps, ACT.Copy)
                    if kind == "fold":
                        last = nc.scalar.activation(fold_hi[:, what * BANK:(what + 1) * BANK], ps, ACT.Copy, scale=SHRINK)
                    if kind == "val":
                        k = 2 * what[0] + what[1]
                        if not isinstance(n, int) or n >= 0 or k >= 4:
                            act.wait_ge(val_stored[k % 4], (n + 1) * 64 + 16 * (k // 4))
                        last = nc.scalar.activation(val_out[k % 4][:, :], ps, ACT.Copy)
                    if kind == "key":
                        g, c = what
                        src = ps.rearrange("k (t z p) -> k t z p", t=HR, z=2)
                        for half in range(2):
                            last = nc.scalar.activation(key_cols(g, half, c, 0), src[0:HALF, :, half, :], ACT.Copy)
                    if kind == "query":
                        g, cc = what
                        if isinstance(n, int) and n < 0:
                            act.wait_ge(pool_fills, 5)
                        act.wait_ge(u1_ready, n + (2 - g))
                        src = ps.rearrange("k (q s z p) -> k q s z p", q=2, s=XR, z=2)
                        for half in range(2):
                            last = nc.scalar.activation(query_cols(g, half, cc, 0), src[0:HALF, :, :, half, :], ACT.Identity,
                                                        bias=u1_head[0:HALF, :], scale=SHRINK)
                    last.then_inc(job_act, 1)

            copy_jobs(-1, PROLOGUE, numbered(PROLOGUE, PRO_BANK)[0])

            def head(n, last):
                slots = LAST if last else BODY
                for slot, jobs in enumerate(numbered(slots)):
                    g = slot - LAG_T
                    if 0 <= g < GROUPS:
                        act.wait_ge(transposed, n * GROUPS + (g + 1))
                        if g >= 2:
                            act.wait_ge(values_done, n * GROUPS + (g - 1))
                        nc.scalar.activation(probT[g % 2][:, :, :], prob_bank.rearrange("j (p i) -> j p i", p=GP),
                                             ACT.Copy).then_inc(probT_done, 1)
                    g = slot - LAG_V
                    if g >= 0:
                        act.wait_ge(values_done, n * GROUPS + (g + 1))
                        if g == 0:
                            act.wait_ge(job_done, jobs_before(n))
                        for f in range(2):
                            last_copy = nc.scalar.activation(att_cols(g, 0, f), att_from(0, f), ACT.Copy)
                        last_copy.then_inc(att_act, 1)
                    copy_jobs(n, slots, jobs)
                    g = slot
                    if g < GROUPS:
                        act.wait_ge(shift_done, n * GROUPS + (g + 1))
                        for p in range(GP):
                            e = prob[g % 4][:, p * TOT:(p + 1) * TOT]
                            last_exp = nc.scalar.activation(e, e, ACT.Exp, bias=shift[:, g % 4, p:p + 1], scale=EXP_SCALE,
                                                            accum_out=total[:, g % 4, p:p + 1])
                        last_exp.then_inc(exp_done, 1)

            with act.Fori(0, NH - 1) as n:
                head(n, False)
            head(NH - 1, True)

        @block.vector
        def _(dve):
            nc.vector.memset(fold_hi[:, NB * TOT:].bitcast(F32), 0.0).then_inc(dve_fills, 1)
            nc.vector.memset(fold_lo[:, NB * TOT:].bitcast(F32), 0.0).then_inc(dve_fills, 1)
            nc.vector.memset(u2r[:, TOT:], -1.0).then_inc(dve_fills, 1)
            dve.wait_ge(setup_loaded, 16 * SETUP_LOADS)
            nc.vector.tensor_copy(wr_twice.rearrange("m (b z d) -> m b z d", z=2, d=D),
                                  wr_raw.rearrange("m (b d) -> m b d", d=D).unsqueeze(2).to_broadcast([128, NB, 2, D])).then_inc(weights_high, 1)
            nc.vector.tensor_copy(wk_hi[:, :], wk_raw).then_inc(weights_high, 1)
            nc.vector.tensor_copy(wv_hi[:, :], wv_raw).then_inc(weights_high, 1)
            dve.wait_ge(weights_high, 3)
            nc.vector.tensor_tensor(wk_lo[:, :], wk_raw, wk_hi[:, :].bitcast(F32), ALU.subtract)
            nc.vector.tensor_tensor(wv_lo[:, :], wv_raw, wv_hi[:, :].bitcast(F32), ALU.subtract).then_inc(weights_split, 1)

            def copy_jobs(n, slots, jobs):
                for at, bank, kind, what in jobs:
                    if kind not in ON_DVE:
                        continue
                    ps = job_bank[bank]
                    dve.wait_ge(job_done, jobs_before(n) + (at + 1))
                    if kind in ("tokens", "fold"):
                        dve.wait_ge(job_act, act_before(n) + count(slots, ON_ACT, at + 1))
                    if kind == "tokens" and what == 0:
                        last = nc.vector.tensor_tensor(xT_lo[:, :], ps, xT_hi[:, :].bitcast(F32), ALU.subtract)
                    if kind == "tokens" and what > 0:
                        part = slice((what - 1) * BANK, what * BANK)
                        last = nc.vector.tensor_tensor(hT_lo[:, part], ps, hT_hi[:, part].bitcast(F32), ALU.subtract)
                    if kind == "fold":
                        part = slice(what * BANK, (what + 1) * BANK)
                        last = nc.vector.scalar_tensor_tensor(out=fold_lo[:, part], in0=ps, scalar=SHRINK,
                                                              in1=fold_hi[:, part].bitcast(F32), op0=ALU.mult, op1=ALU.subtract)
                    if kind == "pos":
                        s, ag = what
                        k = s + XR * ag
                        if k == 0:
                            dve.wait_ge(u2r_loaded, (n + 1) * 16 + 16)
                        if not isinstance(n, int) or n >= 0 or k >= 4:
                            dve.wait_ge(pos_stored[k % 4], (n + 1) * 64 + 16 * (k // 4))
                        last = nc.vector.tensor_tensor(pos_out[k % 4][:, :].rearrange("b (a j) -> b a j", j=TOT),
                                                       ps.rearrange("b (a j) -> b a j", j=TOT),
                                                       window(u2r, WIN, SEG - 1 - 16 * s - 4 * ag, -1), ALU.add)
                    if kind == "key":
                        g, c = what
                        src = ps.rearrange("k (t z p) -> k t z p", t=HR, z=2)
                        for half in range(2):
                            last = nc.vector.tensor_copy(key_cols(g, half, c, 1), src[HALF:, :, half, :])
                    if kind == "query":
                        g, cc = what
                        dve.wait_ge(u1_ready, n + (2 - g))
                        if isinstance(n, int) and n < 0:
                            dve.wait_ge(pool_fills, 5)
                        src = ps.rearrange("k (q s z p) -> k q s z p", q=2, s=XR, z=2)
                        for half in range(2):
                            last = nc.vector.tensor_scalar(query_cols(g, half, cc, 1), src[HALF:, :, :, half, :], SHRINK,
                                                           u1_head[HALF:, :], ALU.mult, ALU.add)
                    if kind == "out":
                        dve.wait_ge(res_loaded, n * 16 + 16)
                        dve.wait_ge(y_stored, n * 16 + 16)
                        last = nc.vector.tensor_tensor(y[:, :], ps, x_res[:, :], ALU.add)
                    last.then_inc(job_dve, 1)

            copy_jobs(-1, PROLOGUE, numbered(PROLOGUE, PRO_BANK)[0])

            def row_weights(n, g):
                dve.wait_ge(exp_done, n * GROUPS + (g + 1))
                nc.vector.reciprocal(inverse[:, g % 4, :], total[:, g % 4, :]).then_inc(inverse_done, 1)
                dve.wait_ge(inverse_done, n * GROUPS + (g + 1))
                nc.vector.tensor_tensor(weight[:, g % 4, :], inverse[:, g % 4, :], mask_i[:, GP * g:GP * (g + 1)],
                                        ALU.mult).then_inc(weight_done, 1)

            def head(n, last):
                slots = LAST if last else BODY
                for slot, jobs in enumerate(numbered(slots)):
                    g = slot
                    if g < GROUPS:
                        s = prob[g % 4][:, :]
                        s3 = s.rearrange("k (p j) -> k p j", j=TOT)
                        dve.wait_ge(scores_done, n * GROUPS + (g + 1))
                        dve.wait_ge(pos_loaded[g % 4], n * 128 + 32 * (g // 4 + 1))
                        if g >= 4:
                            dve.wait_ge(transposed, n * GROUPS + (g - 3))
                        nc.vector.tensor_tensor(s, score_bank[g % 2], pos_in[g % 4][:, :], ALU.add).then_inc(scores_added, 1)
                        dve.wait_ge(scores_added, n * GROUPS + (g + 1))
                        nc.vector.scalar_tensor_tensor(out=s, in0=s, scalar=0.0, in1=s, op0=ALU.is_equal,
                                                       op1=ALU.subtract).then_inc(scores_marked, 1)
                        dve.wait_ge(scores_marked, n * GROUPS + (g + 1))
                        nc.vector.tensor_reduce(least[:, g % 4, :], s3, AX.X, ALU.min).then_inc(least_done, 1)
                        dve.wait_ge(least_done, n * GROUPS + (g + 1))
                        nc.vector.tensor_scalar(shift[:, g % 4, :], least[:, g % 4, :], -EXP_SCALE, None, ALU.mult).then_inc(shift_done, 1)
                    if 1 <= slot <= GROUPS:
                        row_weights(n, slot - 1)
                    g = slot - LAG_V
                    if g >= 0:
                        dve.wait_ge(values_done, n * GROUPS + (g + 1))
                        if g == 0:
                            dve.wait_ge(job_done, jobs_before(n))
                        for f in range(2):
                            last_copy = nc.vector.tensor_copy(att_cols(g, 1, f), att_from(1, f))
                        last_copy.then_inc(att_dve, 1)
                    copy_jobs(n, slots, jobs)
                dve.wait_ge(job_dve, dve_before(n) + count(slots, ON_DVE))
                for s in range(XR):
                    last_stats = nc.vector.bn_stats(stats[:, s, :], y[:, s * MODEL:(s + 1) * MODEL])
                last_stats.then_inc(stats_done, 1)
                dve.wait_ge(dve_fills, 3)
                dve.wait_ge(stats_done, n + 1)
                for s in range(XR):
                    last_aggr = nc.vector.bn_aggr(mean_var[:, s, :], stats[:, s, :])
                last_aggr.then_inc(aggr_done, 1)

            with dve.Fori(0, NH - 1) as n:
                head(n, False)
            head(NH - 1, True)

        @block.tensor
        def _(pe):
            def product(dst, lhs, rhs):
                nc.tensor.matmul(dst, lhs[0], rhs[0], start=True, stop=False)
                nc.tensor.matmul(dst, lhs[0], rhs[1], start=False, stop=False)
                return nc.tensor.matmul(dst, lhs[1], rhs[0], start=False, stop=True)

            pe.wait_ge(setup_loaded, 16 * SETUP_LOADS)
            pe.wait_ge(ident_ready, 1)
            for c in range(NC):
                nc.tensor.transpose(psum[:, c // 4, 128 * (c % 4):128 * (c % 4 + 1)], wq[:, 128 * c:128 * (c + 1)], ident[:, :])
            nc.tensor.transpose(psum[:, 2, 0:128], R_tok, ident[:, :])
            nc.tensor.transpose(psum[:, 2, 128:144], u1_rows, ident[0:NH, 0:NH])
            nc.tensor.transpose(psum[:, 2, 144:160], u2_rows, ident[0:NH, 0:NH])
            nc.tensor.transpose(psum[0:SEG, 2, 160:288], mask_tok, ident[:, :]).then_inc(setup_products, 1)
            pe.wait_ge(setup_copied, 1)
            pe.wait_ge(weights_high, 1)
            for b in range(NB):
                last = nc.tensor.matmul(psum[:, 4 + b // 4, 128 * (b % 4):128 * (b % 4 + 1)], wr_twice[:, 128 * b:128 * (b + 1)],
                                        RT, start=True, stop=True)
            last.then_inc(setup_products, 1)
            pe.wait_ge(setup_copied, 2)
            for n in range(NH):
                last = nc.tensor.matmul(psum[0:1, n // 4, 128 * (n % 4):128 * (n % 4 + 1)], u2T[0:D, n:n + 1],
                                        rT[0:D, n * TOT:(n + 1) * TOT], start=True, stop=True)
            last.then_inc(setup_products, 1)
            pe.wait_ge(weights_split, 1)
            pe.wait_ge(pool_fills, 5)
            pe.wait_ge(dve_fills, 3)

            x_parts = xT_hi, xT_lo
            h_parts = hT_hi, hT_lo

            def do_jobs(n, slots, jobs):
                order = sum(slots, [])
                for at, bank, kind, what in jobs:
                    ps = job_bank[bank]
                    if at >= RINGS:
                        pe.wait_ge(job_act, act_before(n) + count(slots, ON_ACT, at - RINGS + 1)) \
                            if count(slots, ON_ACT, at - RINGS + 1) else None
                        pe.wait_ge(job_dve, dve_before(n) + count(slots, ON_DVE, at - RINGS + 1)) \
                            if count(slots, ON_DVE, at - RINGS + 1) else None

                    def copied(job):
                        end = order.index(job) + 1
                        pe.wait_ge(job_act, act_before(n) + count(slots, ON_ACT, end))
                        pe.wait_ge(job_dve, dve_before(n) + count(slots, ON_DVE, end))

                    if kind == "tokens":
                        src = x_tok if what == 0 else h_tok
                        pe.wait_ge(x_loaded if what == 0 else h_loaded, (n + 1) * 16 + 16)
                        first = 0 if what == 0 else 4 * (what - 1)
                        for k in range(4):
                            last = nc.tensor.transpose(ps[:, 128 * k:128 * (k + 1)], src[:, 128 * (first + k):128 * (first + k + 1)],
                                                       ident[:, :])
                    if kind == "fold":
                        pe.wait_ge(diag_ready, (n + 1) + 1)
                        for q in range(2):
                            last = nc.tensor.matmul(ps[:, 256 * q:256 * (q + 1)], wqT[:, 2 * what + q, :], r_diag[:, :],
                                                    start=True, stop=True)
                    if kind == "pos":
                        s, ag = what
                        if what == (0, 0):
                            copied(FOLD[-1])
                        start = 4 * ag * TOT + SEG - 1 - 16 * s - 4 * ag
                        last = product(ps.rearrange("b (a j) -> b a j", j=TOT),
                                       [part[:, s * B:(s + 1) * B] for part in x_parts],
                                       [window(part, NB * TOT + SEG, start, TOT - 1) for part in (fold_hi, fold_lo)])
                    if kind == "val":
                        t, vh = what
                        last = product(ps, [part[:, t * B:(t + 1) * B] for part in h_parts],
                                       [part[:, vh * BANK:(vh + 1) * BANK] for part in (wv_hi, wv_lo)])
                    if kind == "key":
                        g, c = what
                        last = product(ps.rearrange("k (t z p) -> k t z p", t=HR, z=2),
                                       [part[:, c * 128:(c + 1) * 128] for part in (wk_hi, wk_lo)],
                                       [part[:, :].rearrange("m (t z p) -> m t z p", t=HR, z=2)[:, :, :, HP * g:HP * (g + 1)]
                                        for part in h_parts])
                    if kind == "query":
                        g, cc = what
                        for q in range(2):
                            last = nc.tensor.matmul(ps[:, 256 * q:256 * (q + 1)].rearrange("k (s z p) -> k s z p", s=XR, z=2),
                                                    wq[:, (2 * cc + q) * 128:(2 * cc + q + 1) * 128],
                                                    xT[:, :].rearrange("m (s z p) -> m s z p", s=XR, z=2)[:, :, :, HP * g:HP * (g + 1)],
                                                    start=True, stop=True)
                    if kind == "out":
                        pe.wait_ge(att_act, n * GROUPS + GROUPS)
                        pe.wait_ge(att_dve, n * GROUPS + GROUPS)
                        for s in range(XR):
                            for c in range(NC):
                                last = nc.tensor.matmul(ps[:, MODEL * s:MODEL * (s + 1)], attT[:, c, s, :], mlp[:, c, :],
                                                        start=(c == 0), stop=(c == NC - 1))
                    last.then_inc(job_done, 1)

            do_jobs(-1, PROLOGUE, numbered(PROLOGUE, PRO_BANK)[0])

            def head(n, last):
                slots = LAST if last else BODY
                pe.wait_ge(job_act, act_before(n))
                pe.wait_ge(job_dve, dve_before(n))
                for slot, jobs in enumerate(numbered(slots)):
                    g = slot
                    if g < GROUPS:
                        half = g * GP // HP
                        if g * GP == HP:
                            end = sum(slots, []).index(KEYS[1][-1]) + 1
                            pe.wait_ge(job_act, act_before(n) + count(slots, ON_ACT, end))
                            pe.wait_ge(job_dve, dve_before(n) + count(slots, ON_DVE, end))
                        if g >= 2:
                            pe.wait_ge(scores_added, n * GROUPS + (g - 1))
                        for k in range(GP):
                            p = GP * g - HP * half + k
                            last_mm = nc.tensor.matmul(score_bank[g % 2][:, k * TOT:(k + 1) * TOT],
                                                       q_diag[half][:, 128 * p:128 * (p + 1)],
                                                       kT[half][:, TOT * p:TOT * (p + 1)], start=True, stop=True)
                        last_mm.then_inc(scores_done, 1)
                    g = slot - LAG_T
                    if 0 <= g < GROUPS:
                        pe.wait_ge(prob_done, n * GROUPS + (g + 1))
                        if g >= 1:
                            pe.wait_ge(probT_done, n * GROUPS + g)
                        for k in range(GP):
                            last_mm = nc.tensor.transpose(prob_bank[:, 128 * k:128 * (k + 1)], prob[g % 4][:, TOT * k:TOT * (k + 1)],
                                                          ident[:, :])
                        last_mm.then_inc(transposed, 1)
                    g = slot - LAG_V
                    if g >= 0:
                        pe.wait_ge(probT_done, n * GROUPS + (g + 1))
                        pe.wait_ge(val_loaded[g % 4], n * 128 + 32 * (g // 4 + 1))
                        if g >= 1:
                            pe.wait_ge(att_act, n * GROUPS + g)
                            pe.wait_ge(att_dve, n * GROUPS + g)
                        for k in range(GP):
                            for z in range(2):
                                last_mm = nc.tensor.matmul(att_bank[HALF * z:HALF * (z + 1), SEG * k:SEG * (k + 1)],
                                                           val_in[g % 4][:, z, k, :], probT[g % 2][:, k, SEG * z:SEG * (z + 1)],
                                                           start=True, stop=True)
                        last_mm.then_inc(values_done, 1)
                    do_jobs(n, slots, jobs)

            with pe.Fori(0, NH - 1) as n:
                head(n, False)
            head(NH - 1, True)


_NAMES = ["x", "h", "mask", "w_q", "w_k", "w_v", "w_r", "mlp_w", "u1", "u2", "R", "gamma", "beta"]


def kernel(x, ctx_1024, mask_BxS2_ff1, L0_xattn_w_q, L0_xattn_w_k, L0_xattn_w_v, L0_xattn_w_r, L0_xattn_mlp_w,
           L0_xattn_u1, L0_xattn_u2, L0_xattn_R, L0_xattn_ln_gamma, L0_xattn_ln_beta):
    import numpy as np
    import concourse.bacc as bacc
    from concourse import mybir
    from concourse.bass_utils import run_bass_kernel_spmd

    x = np.asarray(x)
    heads, d = L0_xattn_u1.shape[1], L0_xattn_u1.shape[3]
    given = [x, np.concatenate([np.asarray(ctx_1024), x], axis=1), mask_BxS2_ff1, L0_xattn_w_q, L0_xattn_w_k,
             L0_xattn_w_v, L0_xattn_w_r, L0_xattn_mlp_w, np.reshape(L0_xattn_u1, (heads, d)),
             np.reshape(L0_xattn_u2, (heads, d)), L0_xattn_R, L0_xattn_ln_gamma, L0_xattn_ln_beta]
    nc = bacc.Bacc("TRN2", target_bir_lowering=False, num_devices=1)
    arrays, args = {}, []
    for name, a in zip(_NAMES, given):
        a = np.ascontiguousarray(a)
        arrays[f"in_{name}"] = a
        args.append(nc.dram_tensor(f"in_{name}", a.shape, mybir.dt.from_np(a.dtype), kind="ExternalInput").ap())
    args.append(nc.dram_tensor("out", x.shape, mybir.dt.from_np(x.dtype), kind="ExternalOutput").ap())
    xattn_program(nc, *args)
    result = run_bass_kernel_spmd(nc, [arrays], core_ids=[0])
    return result.results[0]["out"]
```

```python
from contextlib import ExitStack

import concourse.bass as bass
from concourse import mybir


def xattn_program(nc, x, h, mask, w_q, w_k, w_v, w_r, mlp_w, u1, u2, R, gamma, beta, out):
    F32, F32R = mybir.dt.float32, mybir.dt.float32r
    ALU = mybir.AluOpType
    ACT = mybir.ActivationFunctionType
    AX = mybir.AxisListType

    B, SEG, MODEL = x.shape
    TOT = h.shape[1]
    NH, D = u1.shape
    XR, HR = SEG // NH, TOT // NH
    NB = NH * D // D
    NC = NB // 2
    PAIRS = B // 2
    HP = PAIRS // 2
    GP = 4
    GROUPS = PAIRS // GP
    BANK = 512
    HALF = 64
    SHRINK = 2.0**-40
    EXP_SCALE = -(1.0 / SHRINK) / D**0.5
    EPS = 1e-5
    WIN = TOT + SEG

    LAG_T, LAG_V = 3, 4
    FIRST = 6
    OUT_SLOT = GROUPS + LAG_V
    NORM_SLOT = OUT_SLOT + 1
    TOKENS = [("tokens", k) for k in (1, 2, 0)]
    FOLD = [("fold", k) for k in range(4)]
    POS = [("pos", (k % XR, k // XR)) for k in range(16)]
    VAL = [("val", (k // 2, k % 2)) for k in range(16)]
    KEYS = [[("key_act" if c in alone else "key", (g, c)) for c in range(NC)] + [("query", (g, c)) for c in range(NC // 2)]
            for g, alone in enumerate(((1,), (4, 5, 6, 7)))]
    KEYS[1] = KEYS[1][:6] + KEYS[1][8:] + KEYS[1][6:8]
    KEYS_LATE = 4
    OUT = [("out", 0)]

    BLOCK_START = TOKENS + FOLD[:2] + VAL[:1] + FOLD[2:3] + VAL[1:2] + FOLD[3:] + VAL[2:5]
    others = sum(([a, b] for a, b in zip(KEYS[0], VAL[5:])), []) + KEYS[0][11:]
    REST = []
    for k, job in enumerate(POS):
        REST += [job] if k % 5 == 4 else [job, others.pop(0)]
    REST += others
    LOAD_SLOT = GROUPS - 2

    def spread(slots, jobs, over):
        for k, job in enumerate(jobs):
            slots[over[k * len(over) // len(jobs)]].append(job)

    def block_slots(n):
        first = 11 if n == -1 else FIRST
        slots = {i: [] for i in range(first, FIRST + GROUPS)}
        if n == -1:
            slots[11] += TOKENS
            slots[12] += KEYS[0][:NC]
            slots[13] += KEYS[0][NC:] + FOLD + POS
            spread(slots, VAL, range(GROUPS, GROUPS + 2))
            spread(slots, KEYS[1], range(GROUPS + 2, GROUPS + 6))
        elif n is None:
            spread(slots, BLOCK_START[:8], range(FIRST, FIRST + 2))
            spread(slots, BLOCK_START[8:] + REST, range(FIRST + 2, GROUPS))
        if n is None:
            spread(slots, KEYS[1][:-KEYS_LATE], range(GROUPS, OUT_SLOT))
            slots[NORM_SLOT] += KEYS[1][-KEYS_LATE:]
            assert HP // GP <= FIRST + 2 and all(j[0] != "pos" for i in slots if LOAD_SLOT <= i for j in slots[i])
        if n != -1:
            slots[OUT_SLOT] += OUT
        return slots

    PROLOGUE, BODY, LAST = block_slots(-1), block_slots(None), block_slots(NH - 1)
    ON_ACT = ("tokens", "fold", "val", "key", "query", "key_act")
    ON_DVE = ("tokens", "fold", "pos", "key", "query", "out")

    def known(n):
        return isinstance(n, int)

    def stage(n, i, lag):
        g = i - lag
        if g < GROUPS:
            return None if known(n) and n < 0 else (n, g)
        return None if known(n) and n == NH - 1 else (n + 1, g - GROUPS)

    OUT_PLACE = sum(BODY.values(), []).index(OUT[0])

    def part(jobs, k, parts):
        return jobs[k * len(jobs) // parts:(k + 1) * len(jobs) // parts]

    def wait_some(engine, semaphore, count):
        if not known(count) or count > 0:
            engine.wait_ge(semaphore, count)

    def count(slots, kinds, end=None):
        return sum(k in kinds for k, _ in sum(slots.values(), [])[:end])

    ALL = ON_ACT + ON_DVE
    PRO_JOBS, BODY_JOBS = count(PROLOGUE, ALL), count(BODY, ALL)
    PRO_ACT, BODY_ACT = count(PROLOGUE, ON_ACT), count(BODY, ON_ACT)
    PRO_DVE, BODY_DVE = count(PROLOGUE, ON_DVE), count(BODY, ON_DVE)
    RING = 4
    assert BODY_JOBS % RING == 0
    PRO_BANK = -PRO_JOBS % RING

    def jobs_before(n):
        return 0 if known(n) and n < 0 else n * BODY_JOBS + PRO_JOBS

    def act_before(n):
        return 0 if known(n) and n < 0 else n * BODY_ACT + PRO_ACT

    def dve_before(n):
        return 0 if known(n) and n < 0 else n * BODY_DVE + PRO_DVE

    def numbered(slots, first_bank=0):
        at, result = 0, {}
        for i, jobs in slots.items():
            result[i] = [(at + k, (first_bank + at + k) % RING, *job) for k, job in enumerate(jobs)]
            at += len(jobs)
        return result

    def block_of(n):
        return {-1: PROLOGUE, NH - 1: LAST}[n] if known(n) else BODY

    def numbered_block(n):
        return numbered(block_of(n), PRO_BANK if known(n) and n < 0 else 0).items()

    with ExitStack() as ctx:

        def sb(name, shape, dt=F32):
            return ctx.enter_context(nc.sbuf_tensor(name, shape, dt))

        def sem(name):
            return ctx.enter_context(nc.semaphore(name))

        wq = sb("wq", [128, NC * 128])
        wqT = sb("wqT", [128, NC, MODEL])
        wk_hi, wk_lo = sb("wk_hi", [128, NC * 128], F32R), sb("wk_lo", [128, NC * 128], F32R)
        wv_hi, wv_lo = sb("wv_hi", [128, NC * 128], F32R), sb("wv_lo", [128, NC * 128], F32R)
        mlp = sb("mlp", [128, NC, MODEL])
        r_diag = sb("r_diag", [128, 2 * TOT])
        fold_hi, fold_lo = sb("fold_hi", [128, NB * TOT + SEG], F32R), sb("fold_lo", [128, NB * TOT + SEG], F32R)
        u2r = sb("u2r", [128, WIN])
        gamma_b, beta_b = sb("gamma_b", [128, MODEL]), sb("beta_b", [128, MODEL])
        ident = sb("ident", [128, 128])
        u1s, u2T = sb("u1s", [128, NH]), sb("u2T", [128, NH])
        mask_i = sb("mask_i", [128, PAIRS])
        power, epsilon = sb("power", [128, XR]), sb("epsilon", [128, XR])
        minus_scale = sb("minus_scale", [128, GP])
        u1_head = sb("u1_head", [128, 1])
        x_tok, h_tok = sb("x_tok", [128, XR * MODEL]), sb("h_tok", [128, HR * MODEL])
        x_res = sb("x_res", [128, XR * MODEL])
        xT = sb("xT", [128, XR * B])
        xT_hi, xT_lo = sb("xT_hi", [128, XR * B], F32R), sb("xT_lo", [128, XR * B], F32R)
        hT_hi, hT_lo = sb("hT_hi", [128, HR * B], F32R), sb("hT_lo", [128, HR * B], F32R)
        kT = [sb(f"kT{g}", [128, HP * TOT]) for g in range(2)]
        q_diag = [sb(f"q_diag{g}", [128, HP * 128]) for g in range(2)]
        pos_out = [sb(f"pos_out{k}", [128, BANK]) for k in range(4)]
        val_out = [sb(f"val_out{k}", [128, BANK]) for k in range(4)]
        pos_in = [sb(f"pos_in{k}", [128, GP * TOT]) for k in range(4)]
        val_in = [sb(f"val_in{k}", [128, 2, GP, D]) for k in range(4)]
        prob = [sb(f"prob{k}", [128, GP * TOT]) for k in range(4)]
        probT = [sb(f"probT{k}", [128, GP, 128]) for k in range(2)]
        least = sb("least", [128, 4, GP])
        shift = sb("shift", [128, 4, GP])
        total = sb("total", [128, 4, GP])
        inverse = sb("inverse", [128, 4, GP])
        weight = sb("weight", [128, 4, GP])
        attT = sb("attT", [128, NC, XR, B])
        y = sb("y", [128, XR * MODEL])
        stats, mean_var = sb("stats", [128, XR, 6]), sb("mean_var", [128, XR, 2])
        rstd = sb("rstd", [128, XR])

        psum = ctx.enter_context(nc.psum_tensor("psum", [128, 8, BANK], F32))
        score_bank = [psum[:, k, :] for k in range(2)]
        prob_bank = psum[:, 2, :]
        att_bank = psum[:, 3, :]
        job_bank = [psum[:, 4 + k, :] for k in range(RING)]

        pos_dram = nc.dram_tensor("pos_dram", (NH, B, SEG * TOT), F32, kind="Internal").ap()
        val_dram = nc.dram_tensor("val_dram", (NH, B, TOT * D), F32, kind="Internal").ap()
        rT_dram = nc.dram_tensor("rT_dram", (D, NH * TOT), F32, kind="Internal").ap()
        u2r_dram = nc.dram_tensor("u2r_dram", (NH, NH * TOT), F32, kind="Internal").ap()

        setup_space = attT[:, :, :, :].rearrange("k c s b -> k (c s b)")
        wk_raw, wv_raw, wr_raw = (setup_space[:, k * 1024:(k + 1) * 1024] for k in range(3))
        R_tok = setup_space[:, 3072:3200]
        u1_rows, u2_rows = setup_space[0:NH, 3200:3328], setup_space[0:NH, 3328:3456]
        mask_tok = setup_space[:, 3456:3520]
        RT = setup_space[:, 3520:3648]
        u2r_all = kT[1][0:NH, NH * TOT:2 * NH * TOT]
        rT = kT[1][0:D, 0:NH * TOT]

        first_loaded = sem("first_loaded")
        wk_loaded, wv_loaded, mlp_loaded = sem("wk_loaded"), sem("wv_loaded"), sem("mlp_loaded")
        beta_loaded = sem("beta_loaded")
        ident_zero, ident_ready = sem("ident_zero"), sem("ident_ready")
        pool_fills, dve_fills = sem("pool_fills"), sem("dve_fills")
        weights_high, weights_split = sem("weights_high"), sem("weights_split")
        setup_products, setup_copied = sem("setup_products"), sem("setup_copied")
        u2r_stored = sem("u2r_stored")

        x_loaded, h_loaded, u2r_loaded, res_loaded = sem("x_loaded"), sem("h_loaded"), sem("u2r_loaded"), sem("res_loaded")
        rT_stored, diag_loaded = sem("rT_stored"), sem("diag_loaded")
        u1_ready = sem("u1_ready")
        job_done, job_act, job_dve = sem("job_done"), sem("job_act"), sem("job_dve")
        pos_stored, val_stored = [sem(f"pos_stored{k}") for k in range(4)], [sem(f"val_stored{k}") for k in range(4)]
        pos_loaded, val_loaded = [sem(f"pos_loaded{k}") for k in range(4)], [sem(f"val_loaded{k}") for k in range(4)]
        scores_done, scores_added, scores_marked = sem("scores_done"), sem("scores_added"), sem("scores_marked")
        least_done, shift_done, exp_done = sem("least_done"), sem("shift_done"), sem("exp_done")
        inverse_done, weight_done, prob_done = sem("inverse_done"), sem("weight_done"), sem("prob_done")
        transposed, probT_done, values_done = sem("transposed"), sem("probT_done"), sem("values_done")
        att_act, att_dve = sem("att_act"), sem("att_dve")
        stats_done, aggr_done = sem("stats_done"), sem("aggr_done")
        variance_done, rstd_done, centred, norm_done = sem("variance_done"), sem("rstd_done"), sem("centred"), sem("norm_done")
        pool_dmas = sem("pool_dmas")
        FIRST_LOADS = 8

        x_rows = x.rearrange("b s m -> b (s m)")
        h_rows = h.rearrange("b s m -> b (s m)")
        out_rows = out.rearrange("b s m -> b (s m)")

        def rows(array, n, width):
            return array[:, bass.ds(n * width, width)]

        def key_cols(g, half, c, e):
            view = kT[g][HALF * half:HALF * (half + 1), :].rearrange("k (p t c e) -> k p t c e", t=HR, c=NC, e=2)
            return view[:, :, :, c, e].rearrange("k p t -> k t p")

        def query_cols(g, half, cc, f):
            view = q_diag[g][HALF * half:HALF * (half + 1), :].rearrange(
                "k (p z s c q f) -> k p z s c q f", z=2, s=XR, c=NC // 2, q=2, f=2)
            return view[:, :, half, :, cc, :, f].rearrange("k p s q -> k q s p")

        def att_cols(g, half, f):
            b = HALF * half + GP * g
            return attT[HALF * f:HALF * (f + 1), :, :, b:b + GP].rearrange("k a s b -> k b s a")

        def att_from(half, f):
            view = att_bank[HALF * half:HALF * (half + 1), 0:GP * SEG].rearrange("k (b s a f) -> k b s a f", b=GP, s=XR, f=2)
            return view[:, :, :, :, f]

        def window(tile, width, start, step):
            return bass.AP(tile[:, :].tensor, start, [[width, 128], [step, 4], [1, TOT]])

        block = ctx.enter_context(nc.Block())

        @block.sync
        def _(sp):
            def load_tokens(n):
                sp.dma_start(x_tok[:, :], rows(x_rows, n, XR * MODEL)).then_inc(x_loaded, 16)
                sp.dma_start(h_tok[:, :], rows(h_rows, n, HR * MODEL)).then_inc(h_loaded, 16)

            load_tokens(0)
            first_loads = [
                (R_tok, R), (u1_rows[:, 0:D], u1), (u1_rows[:, D:2 * D], u1), (u2_rows[:, 0:D], u2), (u2_rows[:, D:2 * D], u2),
                (mask_tok, mask), (wr_raw, w_r), (wq[:, :], w_q),
            ]
            assert len(first_loads) == FIRST_LOADS
            for dst, src in first_loads:
                sp.dma_start(dst, src).then_inc(first_loaded, 16)
            sp.dma_start(wk_raw, w_k).then_inc(wk_loaded, 16)
            sp.dma_start(wv_raw, w_v).then_inc(wv_loaded, 16)
            sp.dma_start(mlp[:, :, :], mlp_w.rearrange("(c p) m -> p c m", p=128)).then_inc(mlp_loaded, 16)
            sp.dma_start(beta_b[:, :], beta.partition_broadcast(128)).then_inc(beta_loaded, 16)

            u2r_flat = u2r_dram.rearrange("(o n) c -> o (n c)", o=1)

            def load_u2r(n):
                sp.dma_start(u2r[:, 0:TOT], u2r_flat[:, bass.ds(n * (NH + 1) * TOT, TOT)].partition_broadcast(128)).then_inc(u2r_loaded, 16)

            def load_diag(n):
                for half in range(2):
                    sp.dma_start(r_diag[HALF * half:HALF * (half + 1), TOT * half:TOT * (half + 1)],
                                 rT_dram[:, bass.ds(n * TOT, TOT)]).then_inc(diag_loaded, 16)

            def store_jobs(n, slots, jobs):
                for at, _, kind, what in jobs:
                    if kind == "pos":
                        s, ag = what
                        k = s + XR * ag
                        sp.wait_ge(job_dve, dve_before(n) + count(slots, ON_DVE, at + 1))
                        dst = pos_dram[bass.ds(n + 1, 1), :, (16 * s + 4 * ag) * TOT:(16 * s + 4 * ag + 4) * TOT]
                        sp.dma_start(dst.rearrange("o b c -> (o b) c"), pos_out[k % 4][:, :]).then_inc(pos_stored[k % 4], 16)
                    if kind == "val":
                        t, vh = what
                        k = 2 * t + vh
                        sp.wait_ge(job_act, act_before(n) + count(slots, ON_ACT, at + 1))
                        dst = val_dram[bass.ds(n + 1, 1), :, k * BANK:(k + 1) * BANK]
                        sp.dma_start(dst.rearrange("o b c -> (o b) c"), val_out[k % 4][:, :]).then_inc(val_stored[k % 4], 16)

            def load_pos(n, g):
                wait_some(sp, scores_added, n * GROUPS + (g - 3))
                for half in range(2):
                    b = HALF * half + GP * g
                    src = pos_dram[bass.ds(n, 1), b:b + GP, :].rearrange("o p (i j) -> (o i) p j", j=TOT)
                    dst = pos_in[g % 4][HALF * half:HALF * (half + 1), :].rearrange("i (p j) -> i p j", j=TOT)
                    sp.dma_start(dst, src).then_inc(pos_loaded[g % 4], 16)

            def load_val(n, g):
                wait_some(sp, values_done, n * GROUPS + (g - 3))
                for half in range(2):
                    b = HALF * half + GP * g
                    src = val_dram[bass.ds(n, 1), b:b + GP, :].rearrange("o p (j d) -> (o j) p d", d=D)
                    sp.dma_start(val_in[g % 4][:, half, :, :], src).then_inc(val_loaded[g % 4], 16)

            sp.wait_ge(setup_copied, 2)
            sp.dma_start(rT_dram, rT).then_inc(rT_stored, 16)
            sp.wait_ge(pool_fills, 6)
            sp.wait_ge(rT_stored, 16)
            load_diag(0)
            sp.wait_ge(setup_copied, 3)
            sp.dma_start(u2r_dram, u2r_all).then_inc(u2r_stored, 16)
            sp.wait_ge(u2r_stored, 16)
            load_u2r(0)

            def block_program(n, only=None):
                slots = block_of(n)
                for i, jobs in numbered_block(n):
                    if only and i not in only:
                        continue
                    if i == FIRST and slots is not LAST:
                        load_tokens(n + 1)
                        load_diag(n + 1)
                        load_u2r(n + 1)
                    if i == FIRST + 4:
                        sp.dma_start(x_res[:, :], rows(x_rows, n, XR * MODEL)).then_inc(res_loaded, 16)
                    if i == LOAD_SLOT and slots is not LAST:
                        for k in range(4):
                            sp.wait_ge(pos_stored[k], (n + 1) * 64 + 64)
                    if stage(n, i, -2):
                        load_pos(*stage(n, i, -2))
                    if i == GROUPS + 2 and slots is not LAST:
                        for k in range(4):
                            sp.wait_ge(val_stored[k], (n + 1) * 64 + 64)
                    if stage(n, i, 2):
                        load_val(*stage(n, i, 2))
                    store_jobs(n, slots, jobs)

            block_program(-1)
            with sp.Fori(0, NH - 1) as n:
                block_program(n)
            block_program(NH - 1)

        @block.gpsimd
        def _(pool):
            nc.gpsimd.dma_start(gamma_b[:, :], gamma.partition_broadcast(128)).then_inc(pool_dmas, 16)
            nc.gpsimd.memset(ident[:, :], 0.0).then_inc(ident_zero, 1)
            pool.wait_ge(ident_zero, 1)
            nc.gpsimd.affine_select(out=ident[:, :], in_=ident[:, :], compare_op=ALU.not_equal, fill=1.0, base=0,
                                    pattern=[[-1, 128]], channel_multiplier=1).then_inc(ident_ready, 1)
            nc.gpsimd.memset(r_diag[:, :], 0.0).then_inc(pool_fills, 1)
            nc.gpsimd.memset(power[:, :], -0.5).then_inc(pool_fills, 1)
            nc.gpsimd.memset(minus_scale[:, :], -EXP_SCALE).then_inc(pool_fills, 1)
            nc.gpsimd.memset(epsilon[:, :], EPS).then_inc(pool_fills, 1)
            for g in range(2):
                nc.gpsimd.memset(q_diag[g][:, :], 0.0).then_inc(pool_fills, 1)

            def fill_u1(n):
                nc.gpsimd.tensor_copy(u1_head[:, :], u1s[:, bass.ds(n, 1)]).then_inc(u1_ready, 1)

            pool.wait_ge(setup_copied, 1)
            pool.wait_ge(pool_fills, 6)
            pool.wait_ge(pool_dmas, 16)
            fill_u1(0)

            def probabilities(n, g):
                pool.wait_ge(inverse_done, n * GROUPS + (g + 1))
                nc.gpsimd.tensor_tensor(weight[:, g % 4, :], inverse[:, g % 4, :], mask_i[:, GP * g:GP * (g + 1)],
                                        ALU.mult).then_inc(weight_done, 1)
                pool.wait_ge(weight_done, n * GROUPS + (g + 1))
                p = prob[g % 4][:, :].rearrange("k (p j) -> k p j", j=TOT)
                nc.gpsimd.tensor_tensor(p, p, weight[:, g % 4, :].unsqueeze(2).to_broadcast([128, GP, TOT]),
                                        ALU.mult).then_inc(prob_done, 1)

            def shifts(m, g):
                pool.wait_ge(least_done, m * GROUPS + (g + 1))
                nc.gpsimd.tensor_tensor(shift[:, g % 4, :], least[:, g % 4, :], minus_scale[:, :], ALU.mult).then_inc(shift_done, 1)

            def row_rstd(n):
                pool.wait_ge(aggr_done, n + 1)
                nc.gpsimd.tensor_tensor(rstd[:, :], mean_var[:, :, 1], epsilon[:, :], ALU.add).then_inc(variance_done, 1)
                pool.wait_ge(variance_done, n + 1)
                nc.gpsimd.tensor_tensor(rstd[:, :], rstd[:, :], power[:, :], ALU.pow).then_inc(rstd_done, 1)

            def store_output(n):
                pool.wait_ge(norm_done, n + 1)
                nc.gpsimd.dma_start(rows(out_rows, n, XR * MODEL), y[:, :]).then_inc(pool_dmas, 16)

            def block_program(n):
                slots = block_of(n)
                for i in slots:
                    if i == FIRST + 4 and slots is not LAST:
                        fill_u1(n + 1)
                    out_slot = i == OUT_SLOT and slots is not PROLOGUE
                    norm_slot = i == NORM_SLOT and slots is not PROLOGUE
                    if stage(n, i, 0) and not norm_slot:
                        shifts(*stage(n, i, 0))
                    if norm_slot:
                        row_rstd(n)
                    if stage(n, i, 1):
                        probabilities(*stage(n, i, 1))
                    if stage(n, i, -1) and out_slot:
                        shifts(*stage(n, i, -1))
                    if norm_slot:
                        store_output(n)

            block_program(-1)
            with pool.Fori(0, NH - 1) as n:
                block_program(n)
            block_program(NH - 1)
            pool.wait_ge(pool_dmas, 16 * (NH + 1))

        @block.scalar
        def _(act):
            def copy_jobs(n, slots, jobs):
                for at, bank, kind, what in jobs:
                    if kind not in ON_ACT:
                        continue
                    ps = job_bank[bank]
                    act.wait_ge(job_done, jobs_before(n) + (at + 1))
                    if kind == "tokens" and what == 0:
                        nc.scalar.activation(xT[:, :], ps, ACT.Copy)
                        last = nc.scalar.activation(xT_hi[:, :], ps, ACT.Copy)
                    if kind == "tokens" and what > 0:
                        last = nc.scalar.activation(hT_hi[:, (what - 1) * BANK:what * BANK], ps, ACT.Copy)
                    if kind == "fold":
                        last = nc.scalar.activation(fold_hi[:, what * BANK:(what + 1) * BANK], ps, ACT.Copy, scale=SHRINK)
                    if kind == "val":
                        k = 2 * what[0] + what[1]
                        if not known(n) or n >= 0 or k >= 4:
                            act.wait_ge(val_stored[k % 4], (n + 1) * 64 + 16 * (k // 4))
                        last = nc.scalar.activation(val_out[k % 4][:, :], ps, ACT.Copy)
                    if kind in ("key", "key_act"):
                        g, c = what
                        src = ps.rearrange("k (t z p) -> k t z p", t=HR, z=2)
                        for half in range(2):
                            last = nc.scalar.activation(key_cols(g, half, c, 0), src[0:HALF, :, half, :], ACT.Copy)
                        if kind == "key_act":
                            for half in range(2):
                                last = nc.scalar.activation(key_cols(g, half, c, 1), src[HALF:, :, half, :], ACT.Copy)
                    if kind == "query":
                        g, cc = what
                        if known(n) and n < 0:
                            act.wait_ge(pool_fills, 6)
                        act.wait_ge(u1_ready, n + 2)
                        src = ps.rearrange("k (q s z p) -> k q s z p", q=2, s=XR, z=2)
                        for half in range(2):
                            last = nc.scalar.activation(query_cols(g, half, cc, 0), src[0:HALF, :, :, half, :], ACT.Identity,
                                                        bias=u1_head[0:HALF, :], scale=SHRINK)
                    last.then_inc(job_act, 1)

            def transposed_probabilities(n, g):
                act.wait_ge(transposed, n * GROUPS + (g + 1))
                wait_some(act, values_done, n * GROUPS + (g - 1))
                nc.scalar.activation(probT[g % 2][:, :, :], prob_bank.rearrange("j (p i) -> j p i", p=GP),
                                     ACT.Copy).then_inc(probT_done, 1)

            def results(n, g):
                act.wait_ge(values_done, n * GROUPS + (g + 1))
                if g == 0 and (not known(n) or n):
                    act.wait_ge(job_done, jobs_before(n - 1) + OUT_PLACE + 1)
                for f in range(2):
                    last_copy = nc.scalar.activation(att_cols(g, 0, f), att_from(0, f), ACT.Copy)
                last_copy.then_inc(att_act, 1)

            def exponentials(n, g):
                act.wait_ge(shift_done, n * GROUPS + (g + 1))
                for p in range(GP):
                    e = prob[g % 4][:, p * TOT:(p + 1) * TOT]
                    last_exp = nc.scalar.activation(e, e, ACT.Exp, bias=shift[:, g % 4, p:p + 1], scale=EXP_SCALE,
                                                    accum_out=total[:, g % 4, p:p + 1])
                last_exp.then_inc(exp_done, 1)

            def block_program(n, only=None):
                slots = block_of(n)
                for i, jobs in numbered_block(n):
                    if only and i not in only:
                        continue
                    out_slot = i == OUT_SLOT and slots is not PROLOGUE
                    norm_slot = i == NORM_SLOT and slots is not PROLOGUE
                    if not out_slot:
                        copy_jobs(n, slots, part(jobs, 0, 3))
                    if stage(n, i, LAG_T):
                        transposed_probabilities(*stage(n, i, LAG_T))
                    if not out_slot:
                        copy_jobs(n, slots, part(jobs, 1, 3))
                    if out_slot:
                        if stage(n, i, 0):
                            exponentials(*stage(n, i, 0))
                            exponentials(*stage(n, i, -1))
                    if stage(n, i, LAG_V):
                        results(*stage(n, i, LAG_V))
                    if not out_slot:
                        copy_jobs(n, slots, part(jobs, 2, 3))
                        if stage(n, i, 0) and not norm_slot:
                            exponentials(*stage(n, i, 0))

            block_program(-1, range(11, 12))
            act.wait_ge(setup_products, 1)
            for k in range(2):
                nc.scalar.activation(wqT[:, 4 * k:4 * k + 4, :], psum[:, k, :].rearrange("k (c m) -> k c m", c=4), ACT.Copy)
            nc.scalar.activation(RT, psum[:, 2, 0:128], ACT.Copy)
            nc.scalar.activation(u1s[:, :], psum[:, 2, 128:144], ACT.Copy, scale=SHRINK)
            nc.scalar.activation(u2T[:, :], psum[:, 2, 144:160], ACT.Copy)
            for half in range(2):
                last = nc.scalar.activation(mask_i[HALF * half:HALF * (half + 1), :],
                                            psum[0:SEG, 2, 160 + HALF * half:160 + HALF * (half + 1)], ACT.Copy)
            last.then_inc(setup_copied, 1)
            act.wait_ge(setup_products, 2)
            for k in range(4):
                dst = rT.rearrange("k (x b) -> k x b", b=NB)[:, :, 4 * k:4 * k + 4]
                last = nc.scalar.activation(dst, psum[0:D, k, :].rearrange("k (b x) -> k x b", b=4), ACT.Copy)
            last.then_inc(setup_copied, 1)
            block_program(-1, range(12, 13))
            act.wait_ge(setup_products, 3)
            for k in range(4):
                last = nc.scalar.activation(u2r_all[:, k * BANK:(k + 1) * BANK], psum[0:NH, k, :], ACT.Copy, scale=SHRINK)
            last.then_inc(setup_copied, 1)

            block_program(-1, range(13, FIRST + GROUPS))
            with act.Fori(0, NH - 1) as n:
                block_program(n)
            block_program(NH - 1)

        @block.vector
        def _(dve):
            nc.vector.memset(fold_hi[:, NB * TOT:].bitcast(F32), 0.0).then_inc(dve_fills, 1)
            nc.vector.memset(fold_lo[:, NB * TOT:].bitcast(F32), 0.0).then_inc(dve_fills, 1)
            nc.vector.memset(u2r[:, TOT:], -1.0).then_inc(dve_fills, 1)
            def copy_jobs(n, slots, jobs):
                for at, bank, kind, what in jobs:
                    if kind not in ON_DVE or kind == "out":
                        continue
                    ps = job_bank[bank]
                    dve.wait_ge(job_done, jobs_before(n) + (at + 1))
                    if kind in ("tokens", "fold"):
                        dve.wait_ge(job_act, act_before(n) + count(slots, ON_ACT, at + 1))
                    if kind == "tokens" and what == 0:
                        last = nc.vector.tensor_tensor(xT_lo[:, :], ps, xT_hi[:, :].bitcast(F32), ALU.subtract)
                    if kind == "tokens" and what > 0:
                        part = slice((what - 1) * BANK, what * BANK)
                        last = nc.vector.tensor_tensor(hT_lo[:, part], ps, hT_hi[:, part].bitcast(F32), ALU.subtract)
                    if kind == "fold":
                        part = slice(what * BANK, (what + 1) * BANK)
                        last = nc.vector.scalar_tensor_tensor(out=fold_lo[:, part], in0=ps, scalar=SHRINK,
                                                              in1=fold_hi[:, part].bitcast(F32), op0=ALU.mult, op1=ALU.subtract)
                    if kind == "pos":
                        s, ag = what
                        k = s + XR * ag
                        if k == 0:
                            dve.wait_ge(u2r_loaded, (n + 1) * 16 + 16)
                        if not known(n) or n >= 0 or k >= 4:
                            dve.wait_ge(pos_stored[k % 4], (n + 1) * 64 + 16 * (k // 4))
                        last = nc.vector.tensor_tensor(pos_out[k % 4][:, :].rearrange("b (a j) -> b a j", j=TOT),
                                                       ps.rearrange("b (a j) -> b a j", j=TOT),
                                                       window(u2r, WIN, SEG - 1 - 16 * s - 4 * ag, -1), ALU.add)
                    if kind in ("key", "key_act"):
                        g, c = what
                        src = ps.rearrange("k (t z p) -> k t z p", t=HR, z=2)
                        for half in range(2):
                            last = nc.vector.tensor_copy(key_cols(g, half, c, 1), src[HALF:, :, half, :])
                    if kind == "query":
                        g, cc = what
                        dve.wait_ge(u1_ready, n + 2)
                        if known(n) and n < 0:
                            dve.wait_ge(pool_fills, 6)
                        src = ps.rearrange("k (q s z p) -> k q s z p", q=2, s=XR, z=2)
                        for half in range(2):
                            last = nc.vector.tensor_scalar(query_cols(g, half, cc, 1), src[HALF:, :, :, half, :], SHRINK,
                                                           u1_head[HALF:, :], ALU.mult, ALU.add)
                    last.then_inc(job_dve, 1)

            def output(n, slots):
                (at, bank, _, _), = numbered(slots)[OUT_SLOT]
                dve.wait_ge(job_done, jobs_before(n) + (at + 1))
                dve.wait_ge(res_loaded, n * 16 + 16)
                dve.wait_ge(pool_dmas, n * 16 + 16)
                nc.vector.tensor_tensor(y[:, :], job_bank[bank], x_res[:, :], ALU.add).then_inc(job_dve, 1)

            def output_statistics(n, slots):
                dve.wait_ge(job_dve, dve_before(n) + count(slots, ON_DVE, numbered(slots)[OUT_SLOT][0][0] + 1))
                for s in range(XR):
                    last_stats = nc.vector.bn_stats(stats[:, s, :], y[:, s * MODEL:(s + 1) * MODEL])
                last_stats.then_inc(stats_done, 1)
                dve.wait_ge(dve_fills, 3)
                dve.wait_ge(stats_done, n + 1)
                for s in range(XR):
                    last_aggr = nc.vector.bn_aggr(mean_var[:, s, :], stats[:, s, :])
                last_aggr.then_inc(aggr_done, 1)

            def normalise(n):
                dve.wait_ge(beta_loaded, 16)
                dve.wait_ge(rstd_done, n + 1)
                for s in range(XR):
                    row = y[:, s * MODEL:(s + 1) * MODEL]
                    last = nc.vector.scalar_tensor_tensor(out=row, in0=row, scalar=mean_var[:, s, 0:1], in1=gamma_b[:, :],
                                                          op0=ALU.subtract, op1=ALU.mult)
                last.then_inc(centred, 1)
                dve.wait_ge(centred, n + 1)
                for s in range(XR):
                    row = y[:, s * MODEL:(s + 1) * MODEL]
                    last = nc.vector.scalar_tensor_tensor(out=row, in0=row, scalar=rstd[:, s:s + 1], in1=beta_b[:, :],
                                                          op0=ALU.mult, op1=ALU.add)
                last.then_inc(norm_done, 1)

            def scores(n, g):
                s = prob[g % 4][:, :]
                s3 = s.rearrange("k (p j) -> k p j", j=TOT)
                dve.wait_ge(scores_done, n * GROUPS + (g + 1))
                dve.wait_ge(pos_loaded[g % 4], n * 128 + 32 * (g // 4 + 1))
                wait_some(dve, transposed, n * GROUPS + (g - 3))
                nc.vector.tensor_tensor(s, score_bank[g % 2], pos_in[g % 4][:, :], ALU.add).then_inc(scores_added, 1)
                dve.wait_ge(scores_added, n * GROUPS + (g + 1))
                nc.vector.scalar_tensor_tensor(out=s, in0=s, scalar=0.0, in1=s, op0=ALU.is_equal,
                                               op1=ALU.subtract).then_inc(scores_marked, 1)
                dve.wait_ge(scores_marked, n * GROUPS + (g + 1))
                nc.vector.tensor_reduce(least[:, g % 4, :], s3, AX.X, ALU.min).then_inc(least_done, 1)

            def row_sums(n, g):
                dve.wait_ge(exp_done, n * GROUPS + (g + 1))
                nc.vector.reciprocal(inverse[:, g % 4, :], total[:, g % 4, :]).then_inc(inverse_done, 1)

            def results(n, g):
                dve.wait_ge(values_done, n * GROUPS + (g + 1))
                if g == 0 and (not known(n) or n):
                    dve.wait_ge(job_done, jobs_before(n - 1) + OUT_PLACE + 1)
                for f in range(2):
                    last_copy = nc.vector.tensor_copy(att_cols(g, 1, f), att_from(1, f))
                last_copy.then_inc(att_dve, 1)

            def block_program(n, only=None):
                slots = block_of(n)
                for i, jobs in numbered_block(n):
                    if only and i not in only:
                        continue
                    out_slot = i == OUT_SLOT and slots is not PROLOGUE
                    norm_slot = i == NORM_SLOT and slots is not PROLOGUE
                    if stage(n, i, 0) and not norm_slot:
                        scores(*stage(n, i, 0))
                    if norm_slot:
                        output_statistics(n, slots)
                    if not out_slot:
                        copy_jobs(n, slots, part(jobs, 0, 2))
                    if stage(n, i, 1):
                        row_sums(*stage(n, i, 1))
                    if out_slot and stage(n, i, 0):
                        scores(*stage(n, i, -1))
                    if stage(n, i, LAG_V):
                        results(*stage(n, i, LAG_V))
                    if not out_slot:
                        copy_jobs(n, slots, part(jobs, 1, 2))
                    if out_slot:
                        output(n, slots)
                    if norm_slot:
                        normalise(n)

            block_program(-1, range(11, 12))
            dve.wait_ge(wk_loaded, 16)
            nc.vector.tensor_copy(wk_hi[:, :], wk_raw).then_inc(weights_high, 1)
            dve.wait_ge(weights_high, 1)
            nc.vector.tensor_tensor(wk_lo[:, :], wk_raw, wk_hi[:, :].bitcast(F32), ALU.subtract).then_inc(weights_split, 1)
            block_program(-1, range(12, 13))
            dve.wait_ge(wv_loaded, 16)
            nc.vector.tensor_copy(wv_hi[:, :], wv_raw).then_inc(weights_high, 1)
            dve.wait_ge(weights_high, 2)
            nc.vector.tensor_tensor(wv_lo[:, :], wv_raw, wv_hi[:, :].bitcast(F32), ALU.subtract).then_inc(weights_split, 1)
            block_program(-1, range(13, FIRST + GROUPS))
            with dve.Fori(0, NH - 1) as n:
                block_program(n)
            block_program(NH - 1)

        @block.tensor
        def _(pe):
            def product(dst, lhs, rhs):
                nc.tensor.matmul(dst, lhs[0], rhs[0], start=True, stop=False)
                nc.tensor.matmul(dst, lhs[0], rhs[1], start=False, stop=False)
                return nc.tensor.matmul(dst, lhs[1], rhs[0], start=False, stop=True)

            x_parts = xT_hi, xT_lo
            h_parts = hT_hi, hT_lo

            def bank_free(n, slots, at):
                for semaphore, kinds, before in ((job_act, ON_ACT, act_before(n)), (job_dve, ON_DVE, dve_before(n))):
                    if at >= RING:
                        wait_some(pe, semaphore, before + count(slots, kinds, at - RING + 1))
                    else:
                        after = min(count(block, kinds) - count(block, kinds, jobs - RING + at + 1)
                                    for block, jobs in ((BODY, BODY_JOBS), (PROLOGUE, PRO_JOBS)))
                        wait_some(pe, semaphore, before - after)

            def do_jobs(n, slots, jobs):
                order = sum(slots.values(), [])
                for at, bank, kind, what in jobs:
                    ps = job_bank[bank]
                    bank_free(n, slots, at)

                    def copied(job):
                        end = order.index(job) + 1
                        if end > at - RING + 1:
                            pe.wait_ge(job_act, act_before(n) + count(slots, ON_ACT, end))
                            pe.wait_ge(job_dve, dve_before(n) + count(slots, ON_DVE, end))

                    if kind == "tokens":
                        src = x_tok if what == 0 else h_tok
                        pe.wait_ge(x_loaded if what == 0 else h_loaded, (n + 1) * 16 + 16)
                        first = 0 if what == 0 else 4 * (what - 1)
                        for k in range(4):
                            last = nc.tensor.transpose(ps[:, 128 * k:128 * (k + 1)], src[:, 128 * (first + k):128 * (first + k + 1)],
                                                       ident[:, :])
                    if kind == "fold":
                        pe.wait_ge(diag_loaded, (n + 1) * 32 + 32)
                        for q in range(2):
                            last = nc.tensor.matmul(ps[:, 256 * q:256 * (q + 1)], wqT[:, 2 * what + q, :], r_diag[:, :],
                                                    start=True, stop=True)
                    if kind == "pos":
                        s, ag = what
                        if what == (0, 0):
                            copied(FOLD[-1])
                        start = 4 * ag * TOT + SEG - 1 - 16 * s - 4 * ag
                        last = product(ps.rearrange("b (a j) -> b a j", j=TOT),
                                       [part[:, s * B:(s + 1) * B] for part in x_parts],
                                       [window(part, NB * TOT + SEG, start, TOT - 1) for part in (fold_hi, fold_lo)])
                    if kind == "val":
                        t, vh = what
                        if what == (0, 0):
                            copied(TOKENS[1])
                        last = product(ps, [part[:, t * B:(t + 1) * B] for part in h_parts],
                                       [part[:, vh * BANK:(vh + 1) * BANK] for part in (wv_hi, wv_lo)])
                    if kind in ("key", "key_act"):
                        g, c = what
                        if what == (0, 0):
                            copied(TOKENS[-1])
                        last = product(ps.rearrange("k (t z p) -> k t z p", t=HR, z=2),
                                       [part[:, c * 128:(c + 1) * 128] for part in (wk_hi, wk_lo)],
                                       [part[:, :].rearrange("m (t z p) -> m t z p", t=HR, z=2)[:, :, :, HP * g:HP * (g + 1)]
                                        for part in h_parts])
                    if kind == "query":
                        g, cc = what
                        for q in range(2):
                            last = nc.tensor.matmul(ps[:, 256 * q:256 * (q + 1)].rearrange("k (s z p) -> k s z p", s=XR, z=2),
                                                    wq[:, (2 * cc + q) * 128:(2 * cc + q + 1) * 128],
                                                    xT[:, :].rearrange("m (s z p) -> m s z p", s=XR, z=2)[:, :, :, HP * g:HP * (g + 1)],
                                                    start=True, stop=True)
                    last.then_inc(job_done, 1)

            def output(n, slots):
                (at, bank, _, _), = numbered(slots)[OUT_SLOT]
                bank_free(n, slots, at)
                pe.wait_ge(att_act, n * GROUPS + GROUPS)
                pe.wait_ge(att_dve, n * GROUPS + GROUPS)
                for s in range(XR):
                    for c in range(NC):
                        last = nc.tensor.matmul(job_bank[bank][:, MODEL * s:MODEL * (s + 1)], attT[:, c, s, :], mlp[:, c, :],
                                                start=(c == 0), stop=(c == NC - 1))
                last.then_inc(job_done, 1)

            def scores(n, g):
                half = g * GP // HP
                wait_some(pe, scores_added, n * GROUPS + (g - 1))
                for k in range(GP):
                    p = GP * g - HP * half + k
                    last_mm = nc.tensor.matmul(score_bank[g % 2][:, k * TOT:(k + 1) * TOT],
                                               q_diag[half][:, 128 * p:128 * (p + 1)],
                                               kT[half][:, TOT * p:TOT * (p + 1)], start=True, stop=True)
                last_mm.then_inc(scores_done, 1)

            def transposes(n, g):
                pe.wait_ge(prob_done, n * GROUPS + (g + 1))
                wait_some(pe, probT_done, n * GROUPS + g)
                for k in range(GP):
                    last_mm = nc.tensor.transpose(prob_bank[:, 128 * k:128 * (k + 1)], prob[g % 4][:, TOT * k:TOT * (k + 1)],
                                                  ident[:, :])
                last_mm.then_inc(transposed, 1)

            def values(n, g):
                pe.wait_ge(probT_done, n * GROUPS + (g + 1))
                pe.wait_ge(val_loaded[g % 4], n * 128 + 32 * (g // 4 + 1))
                wait_some(pe, att_act, n * GROUPS + g)
                wait_some(pe, att_dve, n * GROUPS + g)
                for k in range(GP):
                    for z in range(2):
                        last_mm = nc.tensor.matmul(att_bank[HALF * z:HALF * (z + 1), SEG * k:SEG * (k + 1)],
                                                   val_in[g % 4][:, z, k, :], probT[g % 2][:, k, SEG * z:SEG * (z + 1)],
                                                   start=True, stop=True)
                last_mm.then_inc(values_done, 1)

            def block_program(n, only=None):
                slots = block_of(n)
                for i, jobs in numbered_block(n):
                    if only and i not in only:
                        continue
                    if i == GROUPS and slots is not LAST:
                        end = sum(slots.values(), []).index(KEYS[0][-1]) + 1
                        pe.wait_ge(job_act, act_before(n) + count(slots, ON_ACT, end))
                        pe.wait_ge(job_dve, dve_before(n) + count(slots, ON_DVE, end))
                    if i == HP // GP:
                        pe.wait_ge(job_act, act_before(n))
                        pe.wait_ge(job_dve, dve_before(n))

                    out_slot = i == OUT_SLOT and slots is not PROLOGUE
                    norm_slot = i == NORM_SLOT and slots is not PROLOGUE
                    if stage(n, i, 0) and not norm_slot:
                        scores(*stage(n, i, 0))
                    if stage(n, i, LAG_T):
                        transposes(*stage(n, i, LAG_T))
                    if out_slot:
                        if stage(n, i, 0):
                            scores(*stage(n, i, -1))
                        output(n, slots)
                    else:
                        do_jobs(n, slots, part(jobs, 0, 2))
                    if stage(n, i, LAG_V):
                        values(*stage(n, i, LAG_V))
                    if not out_slot:
                        do_jobs(n, slots, part(jobs, 1, 2))

            pe.wait_ge(ident_ready, 1)
            block_program(-1, range(11, 12))
            pe.wait_ge(first_loaded, 16 * FIRST_LOADS)
            for c in range(NC):
                nc.tensor.transpose(psum[:, c // 4, 128 * (c % 4):128 * (c % 4 + 1)], wq[:, 128 * c:128 * (c + 1)], ident[:, :])
            nc.tensor.transpose(psum[:, 2, 0:128], R_tok, ident[:, :])
            nc.tensor.transpose(psum[:, 2, 128:144], u1_rows, ident[0:NH, 0:NH])
            nc.tensor.transpose(psum[:, 2, 144:160], u2_rows, ident[0:NH, 0:NH])
            nc.tensor.transpose(psum[0:SEG, 2, 160:288], mask_tok, ident[:, :]).then_inc(setup_products, 1)
            pe.wait_ge(setup_copied, 1)
            for b in range(NB):
                last = nc.tensor.matmul(psum[0:D, b // 4, 128 * (b % 4):128 * (b % 4 + 1)], wr_raw[:, D * b:D * (b + 1)],
                                        RT, start=True, stop=True)
            last.then_inc(setup_products, 1)
            pe.wait_ge(weights_split, 1)
            block_program(-1, range(12, 13))
            pe.wait_ge(setup_copied, 2)
            for k in range(NH * TOT // BANK):
                last = nc.tensor.matmul(psum[0:NH, k, :], u2T[0:D, :], rT[:, k * BANK:(k + 1) * BANK], start=True, stop=True)
            last.then_inc(setup_products, 1)
            pe.wait_ge(weights_split, 2)
            pe.wait_ge(mlp_loaded, 16)
            pe.wait_ge(pool_fills, 6)
            pe.wait_ge(dve_fills, 3)
            block_program(-1, range(13, FIRST + GROUPS))
            with pe.Fori(0, NH - 1) as n:
                block_program(n)
            block_program(NH - 1)


_NAMES = ["x", "h", "mask", "w_q", "w_k", "w_v", "w_r", "mlp_w", "u1", "u2", "R", "gamma", "beta"]


def kernel(x, ctx_1024, mask_BxS2_ff1, L0_xattn_w_q, L0_xattn_w_k, L0_xattn_w_v, L0_xattn_w_r, L0_xattn_mlp_w,
           L0_xattn_u1, L0_xattn_u2, L0_xattn_R, L0_xattn_ln_gamma, L0_xattn_ln_beta):
    import numpy as np
    import concourse.bacc as bacc
    from concourse import mybir
    from concourse.bass_utils import run_bass_kernel_spmd

    x = np.asarray(x)
    heads, d = L0_xattn_u1.shape[1], L0_xattn_u1.shape[3]
    given = [x, np.concatenate([np.asarray(ctx_1024), x], axis=1), mask_BxS2_ff1, L0_xattn_w_q, L0_xattn_w_k,
             L0_xattn_w_v, L0_xattn_w_r, L0_xattn_mlp_w, np.reshape(L0_xattn_u1, (heads, d)),
             np.reshape(L0_xattn_u2, (heads, d)), L0_xattn_R, L0_xattn_ln_gamma, L0_xattn_ln_beta]
    nc = bacc.Bacc("TRN2", target_bir_lowering=False, num_devices=1)
    arrays, args = {}, []
    for name, a in zip(_NAMES, given):
        a = np.ascontiguousarray(a)
        arrays[f"in_{name}"] = a
        args.append(nc.dram_tensor(f"in_{name}", a.shape, mybir.dt.from_np(a.dtype), kind="ExternalInput").ap())
    args.append(nc.dram_tensor("out", x.shape, mybir.dt.from_np(x.dtype), kind="ExternalOutput").ap())
    xattn_program(nc, *args)
    result = run_bass_kernel_spmd(nc, [arrays], core_ids=[0])
    return result.results[0]["out"]
```
